# Optimizing a Trainium2 kernel written in Bass

```python
import numpy as np
import jax
import jax.numpy as jnp

def _softmax(x, axis=-1):
    return jax.nn.softmax(x, axis=axis)
def _gelu(x):
    return jax.nn.gelu(x, approximate=True)
def _silu(x):
    return jax.nn.silu(x)
def _sigmoid(x):
    return jax.nn.sigmoid(x)
def _layernorm(x, axis=-1, eps=1e-5):
    m = jnp.mean(x, axis=axis, keepdims=True)
    v = jnp.var(x, axis=axis, keepdims=True)
    return (x - m) / jnp.sqrt(v + eps)
def _scatter_add(tgt, idx, src, axis=0):
    return tgt.at[idx].add(src)
def _segment_sum(src, seg, n):
    return jax.ops.segment_sum(src, seg, n)

kernel_name = 'mk_conv_preact_d1_conv_nhwc64_b6db6b'

def setup_inputs(seed: int = 0):
    np.random.seed(seed)
    _w = jnp.asarray
    def _rec_inputs():
        import jax
        import jax.numpy as jnp
        _gk = jax.random.key(seed)
        x = 1.648e-05 + 1 * jax.random.normal(jax.random.fold_in(_gk, 1), (4, 192, 192, 64), jnp.float32)
        return x
    x = _rec_inputs()
    def _L0_conv_setup():
        import jax, jax.numpy as jnp
        import numpy as np
        WS = (8, 8)
        HEADS = 8
        DH = 64
        SHIFT = (4, 4)
        SCALE = DH ** (-0.5)
        key = jax.random.key(seed)
        ks = jax.random.split(key, 5)
        dim = 64
        inner = HEADS * DH
        b, h, w = (4, 192, 192)
        x = jax.random.normal(ks[0], (b, h, w, dim), dtype=jnp.float32)
        Wq = jax.random.normal(ks[1], (dim, inner), dtype=jnp.float32) * dim ** (-0.5)
        Wkv = jax.random.normal(ks[2], (dim, 2 * inner), dtype=jnp.float32) * dim ** (-0.5)
        Wo = jax.random.normal(ks[3], (inner, dim), dtype=jnp.float32) * inner ** (-0.5)
        bo = jnp.zeros((dim,), dtype=jnp.float32)
        seq_l = WS[0] * WS[1]
        pos_emb = jax.random.normal(ks[4], (1, HEADS, seq_l, seq_l), dtype=jnp.float32)
        return {'x': x, 'Wq': Wq, 'Wkv': Wkv, 'Wo': Wo, 'bo': bo, 'pos_emb': pos_emb}
    _L0_conv_all = _L0_conv_setup()
    _L0_conv_in = {k: v for k, v in _L0_conv_all.items() if k in ('Wq', 'Wkv', 'Wo', 'bo', 'pos_emb', )}
    del _L0_conv_all

    return {
        "x": x,
        "L0_conv_Wq": _L0_conv_in["Wq"],
        "L0_conv_Wkv": _L0_conv_in["Wkv"],
        "L0_conv_Wo": _L0_conv_in["Wo"],
        "L0_conv_bo": _L0_conv_in["bo"],
        "L0_conv_pos_emb": _L0_conv_in["pos_emb"],
    }

def reference(x, L0_conv_Wq, L0_conv_Wkv, L0_conv_Wo, L0_conv_bo, L0_conv_pos_emb):
    import jax
    import jax.numpy as jnp
    def _L0_conv_ref(x, Wq, Wkv, Wo, bo, pos_emb):
        import jax, jax.numpy as jnp
        import numpy as np
        WS = (8, 8)
        HEADS = 8
        DH = 64
        SHIFT = (4, 4)
        SCALE = DH ** (-0.5)
        b, h, w, c = x.shape
        L = WS[0] * WS[1]
        if SHIFT[0] > 0:
            x = jnp.roll(x, shift=(-SHIFT[0], -SHIFT[1]), axis=(1, 2))
        nw = b * (h // WS[0]) * (w // WS[1])
        x_inp = x.reshape(nw, L, c)
        q = x_inp @ Wq
        kv = x_inp @ Wkv
        k, v = jnp.split(kv, 2, axis=-1)
        q = q.reshape(nw, HEADS, L, DH) * SCALE
        k = k.reshape(nw, HEADS, L, DH)
        v = v.reshape(nw, HEADS, L, DH)
        sim = jnp.einsum('bhid,bhjd->bhij', q, k) + pos_emb
        attn = jax.nn.softmax(sim, axis=-1)
        out = jnp.einsum('bhij,bhjd->bhid', attn, v)
        out = out.reshape(nw, L, HEADS * DH)
        out = out @ Wo + bo
        out = out.reshape(b, h, w, c)
        if SHIFT[0] > 0:
            out = jnp.roll(out, shift=(SHIFT[0], SHIFT[1]), axis=(1, 2))
        return out

    def _gn(v, G=32, eps=1e-5):
        B_, H_, W_, C_ = v.shape
        g = v.reshape(B_, H_, W_, G, C_ // G)
        m = jnp.mean(g, axis=(1, 2, 4), keepdims=True)
        s = jnp.var(g, axis=(1, 2, 4), keepdims=True)
        return ((g - m) / jnp.sqrt(s + eps)).reshape(v.shape)

    def _ln_c(v, eps=1e-6):
        m = jnp.mean(v, axis=-1, keepdims=True)
        s = jnp.var(v, axis=-1, keepdims=True)
        return (v - m) / jnp.sqrt(s + eps)

    def _ln_t(v, eps=1e-5):
        m = jnp.mean(v, axis=-1, keepdims=True)
        s = jnp.var(v, axis=-1, keepdims=True)
        return (v - m) / jnp.sqrt(s + eps)

    def _to_tokens(v):
        B_, H_, W_, C_ = v.shape
        return v.reshape(B_, H_ * W_, C_)
    def _from_tokens(t, like):
        return t.reshape(like.shape)

    x = x + _L0_conv_ref(_gn(x), L0_conv_Wq, L0_conv_Wkv, L0_conv_Wo, L0_conv_bo, L0_conv_pos_emb)
    return x


_drawn_inputs = setup_inputs


def setup_inputs(seed=0):
    import zlib

    import numpy as np

    out = dict(_drawn_inputs(seed))
    spreads = {'L0_conv_bo': (0.0, 0.1)}
    factors = {}
    for name, (base, spread) in spreads.items():
        noise = np.random.default_rng([zlib.crc32(name.encode()), seed]).standard_normal(out[name].shape)
        drawn = base * np.exp(spread * noise) if base else spread * noise
        out[name] = jnp.asarray(drawn.astype(out[name].dtype))
    for name, factor in factors.items():
        out[name] = (out[name] * factor).astype(out[name].dtype)
    return out
```

```python
import concourse.bass as bass
from concourse import mybir
from contextlib import ExitStack

F32 = mybir.dt.float32
F16 = mybir.dt.float16
ALU = mybir.AluOpType
ACT = mybir.ActivationFunctionType
AX = mybir.AxisListType

P = 128
C = 64
HEADS = 8
DH = 64
L = 64
INNER = HEADS * DH
SLICES = 8
GROUPS = 32
SHIFT = 4
GN_EPS = 1e-5

W_UP = 8.0
WO_UP = 16.0
P_UP = 64.0
SIM_UP = W_UP * W_UP / DH ** -0.5
OUT_DOWN = 1.0 / (P_UP * WO_UP)

TILES = 3
WIN = 2
SETS = 2
STEP_TOK = TILES * WIN * L
U = WIN * HEADS
PROJ = 22
RING = 3
OUT_AFTER = 2
XT = 2


def build(nc, x, wq, wkv, wo, bo, pos, out):
    B, H, W, _ = x.shape
    STEPS = H
    SLOTS = TILES * STEPS
    NIT = STEPS // 2
    IMG_TOK = H * W
    PTOK = IMG_TOK // P
    CHUNK = min(96, PTOK)
    CHUNKS = PTOK // CHUNK
    NCH = B * CHUNKS

    xrow = x.rearrange("b h w c -> (b h) w c")
    orow = out.rearrange("b h w c -> (b h) w c")
    xflat = x.rearrange("b h w c -> b (h w) c")
    v_dram = nc.dram_tensor("v_parts", (2 * TILES * WIN, 4, L, INNER), F16, kind="Internal").ap()

    def ring_before(T):
        n = XT + PROJ + XT
        full = min(T, SLOTS)
        steps, part = full // TILES, full % TILES
        n += PROJ * min(steps, STEPS - 1) + XT * min(steps, STEPS - 2)
        if steps + 1 < STEPS:
            n += [0, 8, 16][part]
        return n + max(0, T - 2)

    def parts_before(T):
        full = min(T, SLOTS)
        steps, part = full // TILES, full % TILES
        return PROJ + PROJ * min(steps, STEPS - 1) + ([0, 8, 16][part] if steps + 1 < STEPS else 0)

    def part_number(T, i):
        return ring_before(T) + i + (T >= 2 and i >= OUT_AFTER)

    def out_number(T):
        return ring_before(T) + (OUT_AFTER if T // TILES + 1 < STEPS and T < SLOTS else 0)

    class Slot:

        def __init__(self, it, u):
            self.it, self.u = it, u
            self.number = 6 * it + u if isinstance(it, int) else None
            self.tile = u % TILES
            self.step_parity = (u // TILES) % 2

        def at(self, f):
            if self.number is not None:
                return f(self.number)
            one, two = f(6 + self.u), f(12 + self.u)
            return self.it * (two - one) + (2 * one - two)

        def has(self, f):
            return f(self.number) if self.number is not None else f(6 + self.u)

        def bank(self, f):
            return (f(self.number) if self.number is not None else f(6 + self.u)) % RING

        def step(self, ahead=0):
            return self.at(lambda T: T // TILES + ahead)

    def wait(eng, sem, slot, f):
        v = slot.at(f)
        if not isinstance(v, int) or v > 0:
            eng.wait_ge(sem, v)

    def waits(eng, slot, *pairs):
        values = [slot.at(f) for _, f in pairs]
        values = [v if isinstance(v, int) else eng.to_reg(v) for v in values]
        for (sem, _), v in zip(pairs, values):
            if not isinstance(v, int) or v > 0:
                eng.wait_ge(sem, v)

    def slots(eng, run):
        for u in range(6):
            run(Slot(0, u))
        with eng.Fori(1, NIT - 1) as it:
            for u in range(6):
                run(Slot(it, u))
        for u in range(8):
            run(Slot(NIT - 1, u))

    def ring_list(tt):
        if tt == 0:
            return [("q", s) for s in range(8)]
        if tt == 1:
            return [("v", i) for i in range(6)] + [("k", 0), ("k", 1)]
        return [("k", s) for s in range(2, 8)]

    in_slots = lambda T: T < SLOTS
    has_next = lambda T: T // TILES + 1 < STEPS and T < SLOTS
    has_next2 = lambda T: T // TILES + 2 < STEPS and T < SLOTS

    ctx = ExitStack()
    with ctx:
        def sb(name, shape, dt):
            return ctx.enter_context(nc.sbuf_tensor(name, shape, dt))

        def pb(name, shape, dt):
            return ctx.enter_context(nc.psum_tensor(name, shape, dt))

        def sem(name):
            return ctx.enter_context(nc.semaphore(name))

        ident = sb("ident", [P, P], F32)
        ident16 = sb("ident16", [P, P], F16)
        ident_up = sb("ident_up", [P, P], F16)
        w_qkv = sb("w_qkv", [P, 2, 3 * INNER], F16)
        w_out = sb("w_out", [P, 2, SLICES, P], F16)
        pos_sb = sb("pos_sb", [P, 2, HEADS * L], F16)
        bo_sb = sb("bo_sb", [P, C], F32)
        gn_tab = sb("gn_tab", [P, 2, STEPS, SETS], F32)
        x_in = sb("x_in", [P, 2, TILES * WIN, C], F32)
        x_res = sb("x_res", [P, 2, TILES * WIN, C], F32)
        x_dup = sb("x_dup", [P, TILES * WIN, 2, C], F32)
        xn = sb("xn", [P, SETS, STEP_TOK], F32)
        xs = sb("xs", [P, SETS, STEP_TOK], F16)
        q_sb = sb("q_sb", [P, TILES, 2, U * L], F16)
        k_sb = sb("k_sb", [P, 2, 2, TILES * U * L], F16)
        v_sb = sb("v_sb", [P, TILES, 4, INNER], F16)
        q_bd = sb("q_bd", [P, TILES, 2 * U, P], F16)
        v_bd = sb("v_bd", [P, TILES, 4 * HEADS, P], F16)
        e_in = sb("e_in", [P, WIN, HEADS, L], F32)
        pe_f = sb("pe_f", [P, WIN, HEADS, L], F32)
        pn_f = sb("pn_f", [P, WIN, HEADS, L], F32)
        half_sum = sb("half_sum", [P, WIN, HEADS, L // 2], F32)
        row_max = sb("row_max", [P, WIN, HEADS], F32)
        row_sum = sb("row_sum", [P, WIN, HEADS], F32)
        row_sum_s = sb("row_sum_s", [P, WIN, HEADS], F32)
        row_inv = sb("row_inv", [P, WIN, HEADS], F32)
        p_hi = sb("p_hi", [P, 2, HEADS, WIN * L], F16)
        p_lo = sb("p_lo", [P, 2, HEADS, WIN * L], F16)
        pt_hi = sb("pt_hi", [P, HEADS, SETS * L], F16)
        pt_lo = sb("pt_lo", [P, HEADS, SETS * L], F16)
        o_hi = sb("o_hi", [P, SLICES, SETS, L], F16)
        o_lo = sb("o_lo", [P, SLICES, SETS, L], F16)
        y_sb = sb("y_sb", [P, 2, TILES * WIN, C], F32)

        ring = [pb(f"ring{i}", [P, 512], F32) for i in range(RING)]
        s_ps = [pb(f"s_ps{i}", [P, HEADS, L], F32) for i in range(WIN)]
        pt_ps = [pb(f"pt_ps{i}", [P, HEADS, P], F16) for i in range(2)]
        o_ps = pb("o_ps", [P, SETS, HEADS // 2, L], F32)

        w_loaded = sem("w_loaded")
        stat_loaded = [sem(f"stat_loaded{i}") for i in range(2)]
        stat_used = sem("stat_used")
        consts_made = sem("consts_made")
        ident_made = sem("ident_made")
        bd_cleared = sem("bd_cleared")
        w_hi_made = sem("w_hi_made")
        w_made = sem("w_made")
        gn_step = sem("gn_step")
        gn_sums = sem("gn_sums")
        std_made = sem("std_made")
        gn_made = sem("gn_made")
        xin_loaded = [sem(f"xin_loaded{i}") for i in range(2)]
        xdup_made = sem("xdup_made")
        xs_hi_made = sem("xs_hi_made")
        xs_made = sem("xs_made")
        xb_made = sem("xb_made")
        ring_filled = sem("ring_filled")
        ring_free = sem("ring_free")
        hi_made = sem("hi_made")
        q_loaded = [sem(f"q_loaded{i}") for i in range(TILES)]
        v_stored = [sem(f"v_stored{i}") for i in range(TILES)]
        v_loaded = [sem(f"v_loaded{i}") for i in range(TILES)]
        s_filled = sem("s_filled")
        max_made = sem("max_made")
        sub_made = sem("sub_made")
        exp_made = sem("exp_made")
        half_made = sem("half_made")
        sum_made = sem("sum_made")
        sum_scaled = sem("sum_scaled")
        inv_made = sem("inv_made")
        norm_made = sem("norm_made")
        ph_made = sem("ph_made")
        pl_made = sem("pl_made")
        pt_filled = sem("pt_filled")
        pt_made = sem("pt_made")
        o_filled = sem("o_filled")
        oh_made = sem("oh_made")
        ol_made = sem("ol_made")
        y_stored = [sem(f"y_stored{i}") for i in range(2)]

        def apart(eng):
            eng.wait_ge(w_loaded, 16)

        def chunk_view(t):
            flat = t[:, :, :, :].rearrange("p a s c -> p (a s c)").bitcast(F32)
            return flat[:, 0:CHUNK * C].rearrange("p (t c) -> p t c", c=C)

        stat_x = [chunk_view(q_bd), chunk_view(v_bd)]
        w_f = sb("w_f", [P, 2 * INNER], F32)
        stats = sb("stats", [P, NCH, GROUPS, 6], F32)
        gn_pv = sb("gn_pv", [P, B, GROUPS, 2], F32)
        gn_mean = sb("gn_mean", [P, B, GROUPS, 2], F32)
        gn_var = sb("gn_var", [P, B, GROUPS, 2], F32)
        gn_dev = sb("gn_dev", [P, B, GROUPS, 2], F32)
        avg = sb("avg", [P, P], F32)
        gn_c = sb("gn_c", [P, 2, B], F32)
        gn_s = sb("gn_s", [P, B], F32)

        block = ctx.enter_context(nc.Block())

        def row_views(t_dram, row, tile_view):
            both = t_dram[bass.ds(row, 2)]
            for r in range(2):
                yield tile_view[:, 2 * r:2 * r + 2, :], both[r, SHIFT:SHIFT + 2 * L, :].rearrange(
                    "(w t) c -> t w c", w=2)
            n = L - SHIFT
            yield tile_view[0:n, 4:6, :], both[:, SHIFT + 2 * L:W, :].rearrange("r t c -> t r c")
            yield tile_view[n:L, 4:6, :], both[:, 0:SHIFT, :].rearrange("r t c -> t r c")

        ROW_DMAS = 4 * SETS * 16

        def first_rows(eng, step):
            rows = [step * 2 + st * 2 * H for st in range(SETS)]
            return [r if isinstance(r, int) else eng.snap(r) for r in rows]

        def move_step(eng, dram, buf, parity, rows, semaphore, store):
            if not isinstance(rows[0], int):
                apart(eng)
            for st in range(SETS):
                for chip, mem in row_views(dram, rows[st], buf[st * L:(st + 1) * L, parity]):
                    if store:
                        eng.dma_start(mem, chip).then_inc(semaphore, 16)
                    else:
                        eng.dma_start(chip, mem).then_inc(semaphore, 16)

        @block.sync
        def _(sp):
            def load(dst, src):
                sp.dma_start(dst, src).then_inc(w_loaded, 16)

            for half in range(2):
                rows = slice(half * C, (half + 1) * C)
                load(w_f[rows, 0:INNER], wq)
            for half in range(2):
                load(pn_f[half * L:(half + 1) * L, 0], pos.rearrange("a h i j -> i (a h) j"))
                load(pe_f[half * L:(half + 1) * L, 0], wo.rearrange("(s d) c -> d s c", d=DH))
            load(bo_sb[:, :], bo.partition_broadcast(P))
            for ch in range(NCH):
                if ch >= 2:
                    sp.wait_ge(stat_used, ch - 1)
                im, part = ch // CHUNKS, ch % CHUNKS
                src = xflat[im].rearrange("(p t) c -> p t c", p=P)[:, part * CHUNK:(part + 1) * CHUNK, :]
                sp.dma_start(stat_x[ch % 2], src).then_inc(stat_loaded[ch % 2], 16)
                if ch == 1:
                    sp.wait_ge(w_made, 1)
                    for half in range(2):
                        load(w_f[half * C:(half + 1) * C, :], wkv)
            for n in range(2):
                move_step(sp, xrow, x_in, n, first_rows(sp, n), xin_loaded[n], False)
            sp.wait_ge(bd_cleared, 1)

            def q_blocks(tile):
                src = q_sb[:, tile].rearrange("p a (u i) -> p (a u) i", i=L)
                for st in range(SETS):
                    r = slice(st * DH, (st + 1) * DH)
                    sp.dma_start(q_bd[r, tile, :, r], src[r]).then_inc(q_loaded[tile], 16)

            def v_store(parity, tile):
                for w in range(WIN):
                    dst = v_dram[(parity * TILES + tile) * WIN + w].rearrange("a t n -> t a n")
                    sp.dma_start(dst, v_sb[w * L:(w + 1) * L, tile]).then_inc(v_stored[tile], 16)

            def v_blocks(parity, tile):
                for w in range(WIN):
                    r = slice(w * DH, (w + 1) * DH)
                    src = v_dram[(parity * TILES + tile) * WIN + w].rearrange(
                        "a (h t) (s d) -> (t s) (a h) d", h=HEADS, s=SLICES)
                    sp.dma_start(v_bd[r, tile, :, r], src).then_inc(v_loaded[tile], 16)

            sp.wait_ge(ring_free, XT + 8)
            for tile in range(TILES):
                q_blocks(tile)
            for tile in range(TILES):
                sp.wait_ge(ring_free, XT + 8 + 2 * (tile + 1))
                v_store(0, tile)
            sp.wait_ge(v_stored[0], 32)
            v_blocks(0, 0)

            def slot(s):
                tt, par = s.tile, s.step_parity
                nxt = 1 - par
                if tt == 0:
                    if s.has(has_next2):
                        rows = first_rows(sp, s.step(2))
                        waits(sp, s, (xb_made, lambda T: T // TILES + 1),
                              (xdup_made, lambda T: T // TILES + 1))
                        move_step(sp, xrow, x_in, par, rows, xin_loaded[par], False)
                    if s.has(in_slots):
                        waits(sp, s, (v_stored[1], lambda T: 32 * (T // TILES + 1)),
                              (o_filled, lambda T: 2 * (T - 1)))
                        v_blocks(par, 1)
                    if s.has(has_next):
                        waits(sp, s, (ring_free, lambda T: part_number(T, 7) + 1),
                              (s_filled, lambda T: 2 * (T + 1)))
                        q_blocks(0)
                if tt == 1:
                    if s.has(in_slots):
                        waits(sp, s, (v_stored[2], lambda T: 32 * (T // TILES + 1)),
                              (o_filled, lambda T: 2 * (T - 1)))
                        v_blocks(par, 2)
                    if s.has(lambda T: T >= 4):
                        rows = first_rows(sp, s.step(-1))
                        waits(sp, s, (ring_free, lambda T: out_number(T) + 1))
                        move_step(sp, orow, y_sb, nxt, rows, y_stored[nxt], True)
                    if s.has(has_next):
                        waits(sp, s, (s_filled, lambda T: 2 * (T + 1)))
                        q_blocks(1)
                        for tile in range(TILES):
                            waits(sp, s, (v_loaded[tile], lambda T: 32 * (T // TILES)),
                                  (ring_free, lambda T: part_number(T, 2 * tile + 1) + 1))
                            v_store(nxt, tile)
                if tt == 2 and s.has(has_next):
                    waits(sp, s, (v_stored[0], lambda T: 32 * (T // TILES + 2)),
                          (o_filled, lambda T: 2 * (T - 1)))
                    v_blocks(nxt, 0)
                    waits(sp, s, (s_filled, lambda T: 2 * (T + 1)))
                    q_blocks(2)

            slots(sp, slot)
            for parity in range(2):
                sp.wait_ge(y_stored[parity], ROW_DMAS * NIT)

        def hi_view(kind, n, par):
            return part_view(kind, n, par, 0)

        def part_view(kind, n, par, part):
            if kind == "q":
                return q_sb[:, :, part, :].rearrange("p a (u s) -> p a u s", s=SLICES)[:, :, :, n]
            if kind == "k":
                return k_sb[:, par, part, :].rearrange("p (u s) -> p u s", s=SLICES)[:, :, n]
            return v_sb[:, n // 2, 2 * part + n % 2, :]

        def o_view(t, hf, st):
            return t[:, :, st, hf * (L // 2):(hf + 1) * (L // 2)]

        def o_src(hf, st):
            return o_ps[:, st, :, :].rearrange("p h (t s) -> p s (h t)", s=SLICES)

        @block.gpsimd
        def _(pool):
            pool.memset(ident[:, :], 0.0).then_inc(ident_made, 1)
            pool.wait_ge(ident_made, 1)
            pool.affine_select(out=ident[:, :], in_=ident[:, :], compare_op=ALU.not_equal, fill=1.0,
                               base=0, pattern=[[-1, P]], channel_multiplier=1).then_inc(ident_made, 1)
            pool.memset(avg[:, :], 1.0 / P).then_inc(consts_made, 1)
            pool.memset(w_out[:, :, :, :].rearrange("p a s c -> p (a s c)"), 0.0).then_inc(consts_made, 1)
            pool.wait_ge(stat_used, NCH)
            pool.memset(q_bd[:, :, :, :].rearrange("p a s c -> p (a s c)").bitcast(F32), 0.0)
            pool.memset(v_bd[:, :, :, :].rearrange("p a s c -> p (a s c)").bitcast(F32), 0.0).then_inc(bd_cleared, 1)

            def low_x():
                return pool.tensor_tensor(xs[C:P, :, :], xn[C:P, :, :], xs[C:P, :, :], ALU.subtract)

            def add_bias(parity):
                pool.tensor_tensor(x_res[:, parity], x_in[:, parity],
                                   bo_sb[:, None, :].broadcast_to([P, TILES * WIN, C]),
                                   ALU.add).then_inc(xb_made, 1)

            pool.wait_ge(w_loaded, 7 * 16)
            pool.wait_ge(xin_loaded[0], ROW_DMAS)
            add_bias(0)
            pool.wait_ge(xb_made, 1)
            pool.wait_ge(bd_cleared, 1)
            pool.wait_ge(xs_hi_made, 1)
            low_x().then_inc(xs_made, 1)
            pool.wait_ge(xs_made, 1)

            def slot(s):
                if not s.has(in_slots):
                    return
                tt, par = s.tile, s.step_parity
                if tt == 0 and s.has(has_next):
                    wait(pool, xs_hi_made, s, lambda T: T // TILES + 2)
                    wait(pool, pl_made, s, lambda T: 2 * T)
                    low_x().then_inc(xs_made, 1)
                    wait(pool, xs_made, s, lambda T: T // TILES + 2)
                for w in range(WIN):
                    wait(pool, exp_made, s, lambda T: 2 * T + w + 1)
                    wait(pool, sum_made, s, lambda T: 2 * (T - 1) + w + 1)
                    pool.tensor_tensor(half_sum[:, w], pe_f[:, w, :, 0:L // 2], pe_f[:, w, :, L // 2:L],
                                       ALU.add).then_inc(half_made, 1)
                for w in range(WIN):
                    wait(pool, inv_made, s, lambda T: 2 * T + w + 1)
                    wait(pool, ph_made, s, lambda T: 2 * (T - 1) + w + 1)
                    wait(pool, pl_made, s, lambda T: 2 * (T - 1) + w + 1)
                    pool.tensor_tensor(pn_f[:, w], pe_f[:, w], row_inv[:, w, :, None].broadcast_to([P, HEADS, L]),
                                       ALU.mult).then_inc(norm_made, 1)
                for w in range(WIN):
                    wait(pool, ph_made, s, lambda T: 2 * T + w + 1)
                    hi = p_hi[:, s.u % 2, :, w * L:(w + 1) * L]
                    lo = p_lo[:, s.u % 2, :, w * L:(w + 1) * L]
                    pool.tensor_tensor(lo, pn_f[:, w], hi, ALU.subtract).then_inc(pl_made, 1)
                if tt == 1 and s.has(has_next):
                    wait(pool, xin_loaded[1 - par], s, lambda T: ROW_DMAS * ((T // TILES + 1) // 2 + 1))
                    wait(pool, ring_free, s, lambda T: out_number(T) + 1 if T >= 2 else 0)
                    add_bias(1 - par)

            slots(pool, slot)

        @block.scalar
        def _(act):
            act.wait_ge(ident_made, 2)
            nc.scalar.activation(ident16[:, :], ident[:, :], ACT.Copy)
            nc.scalar.activation(ident_up[:, :], ident[:, :], ACT.Copy, scale=SIM_UP).then_inc(w_hi_made, 1)
            act.wait_ge(w_loaded, 7 * 16)
            act.wait_ge(consts_made, 2)
            nc.scalar.activation(w_qkv[:, 0, 0:INNER], w_f[:, 0:INNER], ACT.Copy, scale=W_UP)
            nc.scalar.activation(pos_sb[:, 0, :], pn_f[:, 0].rearrange("p h j -> p (h j)"), ACT.Copy)
            for half in range(2):
                r = slice(half * C, (half + 1) * C)
                last = nc.scalar.activation(w_out[r, 0, :, r], pe_f[r, 0], ACT.Copy, scale=WO_UP)
            last.then_inc(w_hi_made, 1)
            act.wait_ge(w_loaded, 9 * 16)
            nc.scalar.activation(w_qkv[:, 0, INNER:3 * INNER], w_f[:, :], ACT.Copy, scale=W_UP).then_inc(w_hi_made, 1)
            act.wait_ge(gn_step, 5)
            nc.scalar.activation(gn_s[:, :], gn_c[:, 1, :], ACT.Sqrt).then_inc(std_made, 1)

            def hi_part(kind, n, par, ring_bank):
                src = ring[ring_bank]
                if kind == "q":
                    return nc.scalar.activation(hi_view(kind, n, par), src[:, 0:STEP_TOK].rearrange(
                        "p (a u) -> p a u", a=TILES), ACT.Copy)
                if kind == "k":
                    return nc.scalar.activation(hi_view(kind, n, par), src[:, 0:STEP_TOK], ACT.Copy)
                return nc.scalar.activation(hi_view(kind, n, par), src[:, :], ACT.Copy, scale=1.0 / W_UP)

            def xs_hi():
                nc.scalar.activation(xs[:, :, :], xn[:, :, :], ACT.Copy).then_inc(xs_hi_made, 1)

            def dup(parity):
                nc.scalar.activation(x_dup[:, :, :, :], x_in[:, parity, :, None, :].broadcast_to(
                    [P, TILES * WIN, 2, C]), ACT.Copy).then_inc(xdup_made, 1)

            act.wait_ge(xin_loaded[0], ROW_DMAS)
            dup(0)
            act.wait_ge(ring_free, XT)
            xs_hi()
            act.wait_ge(xin_loaded[1], ROW_DMAS)
            act.wait_ge(ring_filled, XT)
            dup(1)
            for i, (kind, n) in enumerate(ring_list(0) + ring_list(1) + ring_list(2)):
                act.wait_ge(ring_filled, XT + i + 1)
                hi_part(kind, n, 0, (XT + i) % RING).then_inc(hi_made, 1)
            act.wait_ge(ring_free, XT + PROJ + XT)
            xs_hi()

            def exps(s, w):
                wait(act, sub_made, s, lambda T: 2 * T + w + 1)
                wait(act, norm_made, s, lambda T: 2 * (T - 1) + w + 1)
                nc.scalar.activation(pe_f[:, w], e_in[:, w], ACT.Exp, scale=1.0 / SIM_UP).then_inc(exp_made, 1)

            def p_high(s, w):
                wait(act, norm_made, s, lambda T: 2 * T + w + 1)
                wait(act, pt_filled, s, lambda T: 2 * (T - 2) + 2)
                nc.scalar.activation(p_hi[:, s.u % 2, :, w * L:(w + 1) * L], pn_f[:, w], ACT.Copy).then_inc(ph_made, 1)

            def parts(s, lo, hi):
                nxt = 1 - s.step_parity
                for i, (kind, n) in list(enumerate(ring_list(s.tile)))[lo:hi]:
                    if kind == "q" and n == 0:
                        for tile in range(TILES):
                            wait(act, q_loaded[tile], s, lambda T: 32 * (T // TILES + 1))
                    if kind == "k" and n == 0:
                        wait(act, s_filled, s, lambda T: 2 * (T - 1))
                    if kind == "v" and n % 2 == 0:
                        wait(act, v_stored[n // 2], s, lambda T: 32 * (T // TILES + 1))
                    number = lambda T: part_number(T, i)
                    wait(act, ring_filled, s, lambda T: number(T) + 1)
                    hi_part(kind, n, nxt, s.bank(number)).then_inc(hi_made, 1)

            def o_high(s, hf):
                wait(act, o_filled, s, lambda T: 2 * (T - 1) + hf + 1)
                wait(act, ring_filled, s, lambda T: out_number(T) + 1 if T >= 2 else 0)
                for st in range(SETS):
                    nxt = nc.scalar.activation(o_view(o_hi, hf, st), o_src(hf, st), ACT.Copy)
                nxt.then_inc(oh_made, 1)

            def transposed(s, bank, dst):
                wait(act, pt_filled, s, lambda T: 2 * (T - 1) + bank + 1)
                wait(act, o_filled, s, lambda T: 2 * (T - 1))
                nc.scalar.activation(dst[:, :, :], pt_ps[bank][:, :, :], ACT.Copy).then_inc(pt_made, 1)

            def slot(s):
                live, ahead = s.has(in_slots), s.has(has_next)
                before = s.has(lambda T: 1 <= T <= SLOTS)
                if ahead:
                    parts(s, 0, 2)
                if live:
                    exps(s, 0)
                if ahead:
                    parts(s, 2, 3)
                if live:
                    exps(s, 1)
                if ahead:
                    parts(s, 3, 4)
                if before:
                    transposed(s, 0, pt_hi)
                if ahead:
                    parts(s, 4, 5)
                if before:
                    transposed(s, 1, pt_lo)
                if ahead:
                    parts(s, 5, 6)
                if live:
                    p_high(s, 0)
                if before:
                    o_high(s, 0)
                if ahead:
                    parts(s, 6, 8)
                if live:
                    p_high(s, 1)
                if before:
                    o_high(s, 1)
                if s.tile == 1 and s.has(has_next2):
                    wait(act, xin_loaded[s.step_parity], s, lambda T: ROW_DMAS * ((T // TILES + 2) // 2 + 1))
                    wait(act, ring_filled, s, lambda T: ring_before(T - 1))
                    dup(s.step_parity)
                if s.tile == 2 and s.has(has_next2):
                    wait(act, ring_free, s, lambda T: ring_before(T + 1))
                    xs_hi()

            slots(act, slot)

        @block.vector
        def _(dve):
            dve.wait_ge(w_hi_made, 2)
            nc.vector.scalar_tensor_tensor(out=w_qkv[:, 1, 0:INNER], in0=w_f[:, 0:INNER], scalar=W_UP,
                                           in1=w_qkv[:, 0, 0:INNER], op0=ALU.mult, op1=ALU.subtract)
            nc.vector.tensor_tensor(pos_sb[:, 1, :], pn_f[:, 0].rearrange("p h j -> p (h j)"), pos_sb[:, 0, :],
                                    ALU.subtract)
            for half in range(2):
                r = slice(half * C, (half + 1) * C)
                last = nc.vector.scalar_tensor_tensor(out=w_out[r, 1, :, r], in0=pe_f[r, 0], scalar=WO_UP,
                                                      in1=w_out[r, 0, :, r], op0=ALU.mult, op1=ALU.subtract)
            last.then_inc(w_made, 1)
            dve.wait_ge(w_hi_made, 3)
            nc.vector.scalar_tensor_tensor(out=w_qkv[:, 1, INNER:3 * INNER], in0=w_f[:, :], scalar=W_UP,
                                           in1=w_qkv[:, 0, INNER:3 * INNER], op0=ALU.mult,
                                           op1=ALU.subtract).then_inc(w_made, 1)
            for ch in range(NCH):
                dve.wait_ge(stat_loaded[ch % 2], 16 * (ch // 2 + 1))
                for g in range(GROUPS):
                    last = nc.vector.bn_stats(stats[:, ch, g, :], stat_x[ch % 2][:, :, 2 * g:2 * g + 2])
                last.then_inc(stat_used, 1)
            dve.wait_ge(stat_used, NCH)
            for im in range(B):
                for g in range(GROUPS):
                    last = nc.vector.bn_aggr(gn_pv[:, im, g, :], stats[:, im * CHUNKS:(im + 1) * CHUNKS, g, :])
            last.then_inc(gn_step, 1)
            dve.wait_ge(gn_step, 1)
            shape = [P, B, GROUPS, 2]
            nc.vector.tensor_copy(gn_mean[:, :, :, :], gn_pv[:, :, :, 0:1].broadcast_to(shape))
            nc.vector.tensor_copy(gn_var[:, :, :, :], gn_pv[:, :, :, 1:2].broadcast_to(shape)).then_inc(gn_step, 1)
            dve.wait_ge(gn_sums, 1)
            flat = lambda t: t[:, :, :, :].rearrange("p b g e -> p (b g e)")
            nc.vector.tensor_copy(gn_c[:, 0, :], ring[1][:, 0:B])
            nc.vector.tensor_tensor(flat(gn_dev), flat(gn_mean), ring[0][:, 0:P * B // 1][:, 0:B * C], ALU.subtract).then_inc(gn_step, 1)
            dve.wait_ge(gn_step, 3)
            nc.vector.tensor_tensor(flat(gn_mean), flat(gn_dev), flat(gn_dev), ALU.mult).then_inc(gn_made, 1)
            dve.wait_ge(gn_made, 1)
            nc.vector.tensor_tensor(flat(gn_dev), flat(gn_mean), flat(gn_var), ALU.add).then_inc(gn_step, 1)
            dve.wait_ge(gn_sums, 2)
            nc.vector.tensor_scalar(gn_c[:, 1, :], ring[1][:, 0:B], GN_EPS, None, ALU.add).then_inc(gn_step, 1)
            dve.wait_ge(std_made, 1)
            nc.vector.reciprocal(gn_c[:, 1, :], gn_s[:, :]).then_inc(gn_made, 1)
            dve.wait_ge(gn_made, 2)
            for what in range(2):
                for pair in range(2):
                    for st in range(SETS):
                        col = gn_c[:, what, 2 * st + pair:2 * st + pair + 1]
                        last = nc.vector.tensor_copy(gn_tab[:, what, pair * STEPS // 2:(pair + 1) * STEPS // 2, st],
                                                     col.broadcast_to([P, STEPS // 2]))
            last.then_inc(gn_made, 1)
            dve.wait_ge(gn_made, 3)

            def normalize(piece, bank, step):
                src = ring[bank][:, 0:STEP_TOK].rearrange("p (w t) -> p w t", w=3)
                for st in range(SETS):
                    dst = xn[:, st, piece * 3 * L:(piece + 1) * 3 * L].rearrange("p (w t) -> p w t", w=3)
                    mean, inv = (gn_tab[:, what, bass.ds(step, 1), st] for what in range(2))
                    last = nc.vector.tensor_scalar(dst, src[:, :, st * L:(st + 1) * L], mean, inv,
                                                   ALU.subtract, ALU.mult)
                last.then_inc(ring_free, 1)

            def low_part(kind, n, par, bank):
                src = ring[bank]
                hi, lo = part_view(kind, n, par, 0), part_view(kind, n, par, 1)
                if kind == "q":
                    src = src[:, 0:STEP_TOK].rearrange("p (a u) -> p a u", a=TILES)
                    ins = nc.vector.tensor_tensor(lo, src, hi, ALU.subtract)
                elif kind == "k":
                    ins = nc.vector.tensor_tensor(lo, src[:, 0:STEP_TOK], hi, ALU.subtract)
                else:
                    ins = nc.vector.scalar_tensor_tensor(out=lo, in0=src[:, :], scalar=1.0 / W_UP, in1=hi,
                                                         op0=ALU.mult, op1=ALU.subtract)
                ins.then_inc(ring_free, 1)

            for piece in range(XT):
                dve.wait_ge(ring_filled, piece + 1)
                normalize(piece, piece % RING, 0)
            for i, (kind, n) in enumerate(ring_list(0) + ring_list(1) + ring_list(2)):
                dve.wait_ge(hi_made, i + 1)
                low_part(kind, n, 0, (XT + i) % RING)
            dve.wait_ge(xs_made, 1)
            for piece in range(XT):
                dve.wait_ge(ring_filled, XT + PROJ + piece + 1)
                normalize(piece, (XT + PROJ + piece) % RING, 1)

            def max_sub(s, w):
                wait(dve, s_filled, s, lambda T: 2 * T + w + 1)
                nc.vector.reduce_max(row_max[:, w], s_ps[w][:, :, :], AX.X).then_inc(max_made, 1)
                wait(dve, max_made, s, lambda T: 2 * T + w + 1)
                wait(dve, exp_made, s, lambda T: 2 * (T - 1) + w + 1)
                nc.vector.tensor_tensor(e_in[:, w], s_ps[w][:, :, :], row_max[:, w, :, None].broadcast_to(
                    [P, HEADS, L]), ALU.subtract).then_inc(sub_made, 1)

            def sums(s, w):
                wait(dve, half_made, s, lambda T: 2 * T + w + 1)
                nc.vector.reduce_sum(row_sum[:, w], half_sum[:, w], AX.X).then_inc(sum_made, 1)

            def scaled(s, w):
                wait(dve, sum_made, s, lambda T: 2 * T + w + 1)
                nc.vector.tensor_scalar(row_sum_s[:, w], row_sum[:, w], 1.0 / P_UP, None,
                                        ALU.mult).then_inc(sum_scaled, 1)

            def inverse(s, w):
                wait(dve, sum_scaled, s, lambda T: 2 * T + w + 1)
                nc.vector.reciprocal(row_inv[:, w], row_sum_s[:, w]).then_inc(inv_made, 1)

            def parts(s, which):
                for i in which:
                    kind, n = ring_list(s.tile)[i]
                    wait(dve, hi_made, s, lambda T: parts_before(T) + i + 1)
                    low_part(kind, n, 1 - s.step_parity, s.bank(lambda T: part_number(T, i)))

            def o_low(s, hf):
                wait(dve, oh_made, s, lambda T: 2 * (T - 1) + hf + 1)
                for st in range(SETS):
                    last = nc.vector.tensor_tensor(o_view(o_lo, hf, st), o_src(hf, st), o_view(o_hi, hf, st),
                                                   ALU.subtract)
                last.then_inc(ol_made, 1)

            def finish(s):
                tile = (s.u - 2) % TILES
                par = ((s.u - 2) // TILES) % 2
                wait(dve, ring_filled, s, lambda T: out_number(T) + 1)
                wait(dve, xb_made, s, lambda T: (T - 2) // TILES + 1)
                if tile == 0:
                    wait(dve, y_stored[par], s, lambda T: ROW_DMAS * ((T - 2) // TILES // 2))
                nc.vector.scalar_tensor_tensor(
                    out=y_sb[:, par, 2 * tile:2 * tile + 2, :].rearrange("p w c -> p (w c)"),
                    in0=ring[s.bank(out_number)][:, 0:P], scalar=OUT_DOWN,
                    in1=x_res[:, par, 2 * tile:2 * tile + 2, :].rearrange("p w c -> p (w c)"),
                    op0=ALU.mult, op1=ALU.add).then_inc(ring_free, 1)

            def slot(s):
                live, ahead = s.has(in_slots), s.has(has_next)
                before = s.has(lambda T: 1 <= T <= SLOTS)
                if live:
                    max_sub(s, 0)
                if ahead:
                    parts(s, [0, 1])
                if live:
                    max_sub(s, 1)
                if s.has(lambda T: T >= 2):
                    finish(s)
                if ahead:
                    parts(s, [2])
                if live:
                    sums(s, 0)
                if ahead:
                    parts(s, [3])
                if live:
                    scaled(s, 0)
                if ahead:
                    parts(s, [4])
                if live:
                    inverse(s, 0)
                    sums(s, 1)
                if ahead:
                    parts(s, [5])
                if live:
                    scaled(s, 1)
                if before:
                    o_low(s, 0)
                if live:
                    inverse(s, 1)
                if ahead:
                    parts(s, range(6, len(ring_list(s.tile))))
                if s.tile == 2 and s.has(has_next2):
                    wait(dve, xs_made, s, lambda T: T // TILES + 2)
                    for piece in range(XT):
                        wait(dve, ring_filled, s, lambda T: part_number(T, 6 + piece) + 1)
                        normalize(piece, s.bank(lambda T: part_number(T, 6 + piece)), s.step(2))
                if before:
                    o_low(s, 1)

            slots(dve, slot)

        @block.tensor
        def _(pe):
            mm = nc.tensor.matmul
            pe.wait_ge(consts_made, 1)
            pe.wait_ge(gn_step, 2)
            mean = gn_mean[:, :, :, :].rearrange("p b g e -> p b (g e)")
            dev = gn_dev[:, :, :, :].rearrange("p b g e -> p b (g e)")
            mm(ring[0][:, 0:B * C], avg[:, :], gn_mean[:, :, :, :].rearrange("p b g e -> p (b g e)"),
               start=True, stop=True)
            for t, at in ((mean, 1), (dev, 2)):
                if at == 2:
                    pe.wait_ge(gn_step, 4)
                for im in range(B):
                    for half in range(2):
                        last = mm(ring[1][half * C:(half + 1) * C, im:im + 1], t[:, im, :], avg[:, 0:1],
                                  start=True, stop=True)
                last.then_inc(gn_sums, 1)

            def transpose_x(piece, bank):
                for j in range(3):
                    last = nc.tensor.transpose(ring[bank][:, j * P:(j + 1) * P],
                                               x_dup[:, 3 * piece + j].rearrange("p a c -> p (a c)"), ident[:, :])
                last.then_inc(ring_filled, 1)

            def project(kind, n, bank):
                if kind == "v":
                    tile, st = n // 2, n % 2
                    for part in range(2):
                        last = mm(ring[bank][:, :], xs[:, st, tile * P:(tile + 1) * P],
                                  w_qkv[:, part, 2 * INNER:3 * INNER], start=part == 0, stop=part == 1)
                else:
                    col = (INNER if kind == "k" else 0) + n * DH
                    for part in range(2):
                        for st in range(SETS):
                            last = mm(ring[bank][st * DH:(st + 1) * DH, 0:STEP_TOK],
                                      w_qkv[:, part, col:col + DH], xs[:, st, :],
                                      start=part == 0, stop=part == 1)
                last.then_inc(ring_filled, 1)

            pe.wait_ge(gn_made, 3)
            pe.wait_ge(ident_made, 2)
            pe.wait_ge(xdup_made, 1)
            for piece in range(XT):
                transpose_x(piece, piece % RING)
            pe.wait_ge(w_made, 2)
            pe.wait_ge(xs_made, 1)
            for i, (kind, n) in enumerate(ring_list(0) + ring_list(1) + ring_list(2)):
                pe.wait_ge(ring_free, max(XT, XT + i - RING + 1))
                project(kind, n, (XT + i) % RING)
            pe.wait_ge(xdup_made, 2)
            for piece in range(XT):
                pe.wait_ge(ring_free, XT + PROJ + piece - RING + 1)
                transpose_x(piece, (XT + PROJ + piece) % RING)

            def scores(s, w):
                if w == 0:
                    wait(pe, q_loaded[s.tile], s, lambda T: 32 * (T // TILES + 1))
                    wait(pe, ring_free, s, lambda T: ring_before(T - T % TILES))
                wait(pe, sub_made, s, lambda T: 2 * (T - 1) + w + 1)
                bank = s_ps[w]
                for part in range(2):
                    mm(bank[:, :, :].rearrange("p h j -> p (h j)"), ident_up[:, :], pos_sb[:, part, :],
                       start=part == 0, stop=False)
                for h in range(HEADS):
                    u = w * HEADS + h
                    key = (s.tile * U + u) * L
                    for qp, kp in ((0, 0), (0, 1), (1, 0)):
                        last = mm(bank[:, h, :], q_bd[:, s.tile, qp * U + u, :],
                                  k_sb[:, s.step_parity, kp, key:key + L], start=False,
                                  stop=h == HEADS - 1 and qp == 1)
                last.then_inc(s_filled, 1)

            def output(s):
                wait(pe, ol_made, s, lambda T: 2 * (T - 2) + 2)
                wait(pe, ring_free, s, lambda T: out_number(T) - RING + 1)
                bank = ring[s.bank(out_number)]
                for sl in range(SLICES):
                    for i, (o, part) in enumerate(((o_hi, 0), (o_hi, 1), (o_lo, 0))):
                        last = mm(bank[:, 0:P], o[:, sl].rearrange("p a t -> p (a t)"), w_out[:, part, sl, :],
                                  start=sl == 0 and i == 0, stop=sl == SLICES - 1 and i == 2)
                last.then_inc(ring_filled, 1)

            def parts(s, lo, hi):
                for i, (kind, n) in list(enumerate(ring_list(s.tile)))[lo:hi]:
                    if s.tile == 0 and i == 0:
                        wait(pe, xs_made, s, lambda T: T // TILES + 2)
                    wait(pe, ring_free, s, lambda T: part_number(T, i) - RING + 1)
                    project(kind, n, s.bank(lambda T: part_number(T, i)))

            def transpose_p(s, part):
                par = (s.u - 1) % 2
                wait(pe, pl_made, s, lambda T: 2 * (T - 1) + 2)
                wait(pe, pt_made, s, lambda T: 2 * (T - 2) + part + 1)
                for h in range(HEADS):
                    last = nc.tensor.transpose(pt_ps[part][:, h, :], (p_hi, p_lo)[part][:, par, h, :], ident16[:, :])
                last.then_inc(pt_filled, 1)

            def weigh(s, hf):
                tile = (s.u - 1) % TILES
                if hf == 0:
                    wait(pe, pt_made, s, lambda T: 2 * T)
                    wait(pe, v_loaded[tile], s, lambda T: 32 * ((T - 1) // TILES + 1))
                wait(pe, ol_made, s, lambda T: 2 * (T - 1) + hf)
                for st in range(SETS):
                    for h4 in range(HEADS // 2):
                        h = hf * (HEADS // 2) + h4
                        for i, (vp, p) in enumerate(((0, pt_hi), (0, pt_lo), (1, pt_hi))):
                            last = mm(o_ps[:, st, h4, :], v_bd[:, tile, (2 * vp + st) * HEADS + h, :],
                                      p[:, h, st * L:(st + 1) * L], start=i == 0, stop=i == 2)
                last.then_inc(o_filled, 1)

            def slot(s):
                live, ahead = s.has(in_slots), s.has(has_next)
                before = s.has(lambda T: 1 <= T <= SLOTS)
                if live:
                    scores(s, 0)
                if ahead:
                    parts(s, 0, 2)
                if live:
                    scores(s, 1)
                if s.has(lambda T: T >= 2):
                    output(s)
                if ahead:
                    parts(s, 2, 4)
                if before:
                    transpose_p(s, 0)
                if ahead:
                    parts(s, 4, 5)
                if before:
                    transpose_p(s, 1)
                if ahead:
                    parts(s, 5, 6)
                if before:
                    weigh(s, 0)
                if ahead:
                    parts(s, 6, 8)
                if s.tile == 2 and s.has(has_next2):
                    wait(pe, xdup_made, s, lambda T: T // TILES + 3)
                    for piece in range(XT):
                        wait(pe, ring_free, s, lambda T: part_number(T, 6 + piece) - RING + 1)
                        transpose_x(piece, s.bank(lambda T: part_number(T, 6 + piece)))
                if before:
                    weigh(s, 1)

            slots(pe, slot)


_INS = ["x", "L0_conv_Wq", "L0_conv_Wkv", "L0_conv_Wo", "L0_conv_bo", "L0_conv_pos_emb"]


def kernel(**inputs):
    import numpy as _np
    import concourse.bacc as _bacc
    from concourse import mybir as _mybir
    from concourse.bass_utils import run_bass_kernel_spmd as _run

    nc = _bacc.Bacc("TRN2", target_bir_lowering=False, num_devices=1)
    arrays, args = {}, []
    for name in _INS:
        a = _np.ascontiguousarray(inputs[name])
        arrays[f"in_{name}_dram"] = a
        args.append(nc.dram_tensor(f"in_{name}_dram", a.shape, _mybir.dt.from_np(a.dtype), kind="ExternalInput").ap())
    shape = arrays["in_x_dram"].shape
    args.append(nc.dram_tensor("out_0_dram", shape, _mybir.dt.float32, kind="ExternalOutput").ap())
    build(nc, *args)
    r = _run(nc, [arrays], core_ids=[0])
    return r.results[0]["out_0_dram"]
```

```python
import concourse.bass as bass
from concourse import mybir
from contextlib import ExitStack

F32 = mybir.dt.float32
F16 = mybir.dt.float16
ALU = mybir.AluOpType
ACT = mybir.ActivationFunctionType
AX = mybir.AxisListType

P = 128
C = 64
HEADS = 8
DH = 64
L = 64
INNER = HEADS * DH
SLICES = 8
GROUPS = 32
SHIFT = 4
GN_EPS = 1e-5

W_UP = 8.0
WO_UP = 16.0
P_UP = 64.0
SIM_UP = W_UP * W_UP / DH ** -0.5
OUT_DOWN = 1.0 / (P_UP * WO_UP)

TILES = 3
WIN = 2
SETS = 2
STEP_TOK = TILES * WIN * L
U = WIN * HEADS
PROJ = 22
RING = 3
OUT_AFTER = 3
XT = 2


def build(nc, x, wq, wkv, wo, bo, pos, out):
    B, H, W, _ = x.shape
    STEPS = H
    SLOTS = TILES * STEPS
    NIT = STEPS // 2
    IMG_TOK = H * W
    PTOK = IMG_TOK // P
    CHUNK = min(96, PTOK)
    CHUNKS = PTOK // CHUNK
    NCH = B * CHUNKS

    xrow = x.rearrange("b h w c -> (b h) w c")
    orow = out.rearrange("b h w c -> (b h) w c")
    xflat = x.rearrange("b h w c -> b (h w) c")
    v_dram = nc.dram_tensor("v_parts", (2 * TILES * WIN, 4, L, INNER), F16, kind="Internal").ap()

    def ring_before(T):
        n = XT + PROJ + XT
        full = min(T, SLOTS)
        steps, part = full // TILES, full % TILES
        n += PROJ * min(steps, STEPS - 1) + XT * min(steps, STEPS - 2)
        if steps + 1 < STEPS:
            n += [0, 8, 16][part]
        return n + max(0, T - 2)

    def parts_before(T):
        full = min(T, SLOTS)
        steps, part = full // TILES, full % TILES
        return PROJ + PROJ * min(steps, STEPS - 1) + ([0, 8, 16][part] if steps + 1 < STEPS else 0)

    def part_number(T, i):
        return ring_before(T) + i + (T >= 2 and i >= OUT_AFTER)

    def out_number(T):
        return ring_before(T) + (OUT_AFTER if T // TILES + 1 < STEPS and T < SLOTS else 0)

    class Slot:

        def __init__(self, it, u):
            self.it, self.u = it, u
            self.number = 6 * it + u if isinstance(it, int) else None
            self.tile = u % TILES
            self.step_parity = (u // TILES) % 2
            self.parity = u % 2

        def at(self, f):
            if self.number is not None:
                return f(self.number)
            one, two = f(6 + self.u), f(12 + self.u)
            return self.it * (two - one) + (2 * one - two)

        def has(self, f):
            return f(self.number) if self.number is not None else f(6 + self.u)

        def bank(self, f):
            return (f(self.number) if self.number is not None else f(6 + self.u)) % RING

        def before(self, n):
            return Slot(self.it, self.u - n)

        def step(self, ahead=0):
            return self.at(lambda T: T // TILES + ahead)

    def wait(eng, sem, slot, f):
        v = slot.at(f)
        if not isinstance(v, int) or v > 0:
            eng.wait_ge(sem, v)

    def waits(eng, slot, *pairs):
        values = [slot.at(f) for _, f in pairs]
        values = [v if isinstance(v, int) else eng.to_reg(v) for v in values]
        for (sem, _), v in zip(pairs, values):
            if not isinstance(v, int) or v > 0:
                eng.wait_ge(sem, v)

    def slots(eng, run):
        for u in range(6):
            run(Slot(0, u))
        with eng.Fori(1, NIT - 1) as it:
            for u in range(6):
                run(Slot(it, u))
        for u in range(8):
            run(Slot(NIT - 1, u))

    def ring_list(tt):
        if tt == 0:
            return [("q", s) for s in range(8)]
        if tt == 1:
            return [("v", i) for i in range(6)] + [("k", 0), ("k", 1)]
        return [("k", s) for s in range(2, 8)]

    def k_results(T):
        first = T - T % TILES
        return ring_before(first) - (XT if has_next2(first - 1) else 0)

    in_slots = lambda T: T < SLOTS
    has_next = lambda T: T // TILES + 1 < STEPS and T < SLOTS
    has_next2 = lambda T: T // TILES + 2 < STEPS and T < SLOTS

    ctx = ExitStack()
    with ctx:
        def sb(name, shape, dt):
            return ctx.enter_context(nc.sbuf_tensor(name, shape, dt))

        def pb(name, shape, dt):
            return ctx.enter_context(nc.psum_tensor(name, shape, dt))

        def sem(name):
            return ctx.enter_context(nc.semaphore(name))

        ident = sb("ident", [P, P], F32)
        ident16 = sb("ident16", [P, P], F16)
        pair_up = sb("pair_up", [P, P], F16)
        w_qkv = sb("w_qkv", [P, 2, 3 * INNER], F16)
        w_out = sb("w_out", [P, 2, SLICES, P], F16)
        pos_sb = sb("pos_sb", [P, HEADS * L], F16)
        bo_sb = sb("bo_sb", [P, C], F32)
        gn_tab = sb("gn_tab", [P, 2, 2, C], F32)
        x_in = sb("x_in", [P, 2, TILES * WIN, C], F32)
        x_res = sb("x_res", [P, 2, TILES * WIN, C], F32)
        xc = sb("xc", [P, TILES * WIN, C], F32)
        xn = sb("xn", [P, TILES * WIN, C], F32)
        xh = sb("xh", [P, TILES * WIN, 2, C], F16)
        xs = sb("xs", [P, SETS, STEP_TOK], F16)
        q_sb = sb("q_sb", [P, TILES, 2, U * L], F16)
        k_sb = sb("k_sb", [P, 2, 2, TILES * U * L], F16)
        v_sb = sb("v_sb", [P, TILES, 4, INNER], F16)
        q_bd = sb("q_bd", [P, TILES, 2 * U, P], F16)
        v_bd = sb("v_bd", [P, TILES, 4 * HEADS, P], F16)
        e_in = sb("e_in", [P, WIN, HEADS, L], F32)
        pe_f = sb("pe_f", [P, 2, WIN, HEADS, L], F32)
        pn_f = sb("pn_f", [P, WIN, HEADS, L], F32)
        half_sum = sb("half_sum", [P, WIN, HEADS, L // 2], F32)
        row_max = sb("row_max", [P, WIN, HEADS], F32)
        row_sum = sb("row_sum", [P, WIN, HEADS], F32)
        row_sum_s = sb("row_sum_s", [P, WIN, HEADS], F32)
        row_inv = sb("row_inv", [P, 2, WIN, HEADS], F32)
        p_hi = sb("p_hi", [P, 2, HEADS, WIN * L], F16)
        p_lo = sb("p_lo", [P, 2, HEADS, WIN * L], F16)
        pt_hi = sb("pt_hi", [P, HEADS, SETS * L], F16)
        pt_lo = sb("pt_lo", [P, HEADS, SETS * L], F16)
        o_hi = sb("o_hi", [P, SLICES, SETS, L], F16)
        o_lo = sb("o_lo", [P, SLICES, SETS, L], F16)
        y_sb = sb("y_sb", [P, 2, TILES * WIN, C], F32)

        ring = [pb(f"ring{i}", [P, 512], F32) for i in range(RING)]
        s_ps = [pb(f"s_ps{i}", [P, HEADS, L], F32) for i in range(WIN)]
        pt_ps = [pb(f"pt_ps{i}", [P, HEADS, P], F16) for i in range(2)]
        o_ps = pb("o_ps", [P, SETS, HEADS // 2, L], F32)

        w_loaded = sem("w_loaded")
        stat_loaded = [sem(f"stat_loaded{i}") for i in range(3)]
        stat_used = sem("stat_used")
        consts_made = sem("consts_made")
        ident_made = sem("ident_made")
        bd_cleared = sem("bd_cleared")
        w_hi_made = sem("w_hi_made")
        w_made = sem("w_made")
        gn_step = sem("gn_step")
        gn_sums = sem("gn_sums")
        std_made = sem("std_made")
        gn_made = sem("gn_made")
        xin_loaded = [sem(f"xin_loaded{i}") for i in range(2)]
        xc_made = sem("xc_made")
        xn_made = sem("xn_made")
        x_hi_made = sem("x_hi_made")
        x_lo_made = sem("x_lo_made")
        xb_made = sem("xb_made")
        ring_filled = sem("ring_filled")
        ring_free = sem("ring_free")
        hi_made = sem("hi_made")
        q_loaded = [sem(f"q_loaded{i}") for i in range(TILES)]
        v_stored = [sem(f"v_stored{i}") for i in range(TILES)]
        v_loaded = [sem(f"v_loaded{i}") for i in range(TILES)]
        s_filled = sem("s_filled")
        max_made = sem("max_made")
        sub_made = sem("sub_made")
        exp_made = sem("exp_made")
        half_made = sem("half_made")
        sum_made = sem("sum_made")
        sum_scaled = sem("sum_scaled")
        inv_made = sem("inv_made")
        norm_made = sem("norm_made")
        ph_made = sem("ph_made")
        pl_made = sem("pl_made")
        pt_filled = sem("pt_filled")
        pt_made = sem("pt_made")
        o_filled = sem("o_filled")
        oh_made = sem("oh_made")
        ol_made = sem("ol_made")
        y_stored = [sem(f"y_stored{i}") for i in range(2)]

        def apart(eng):
            eng.wait_ge(w_loaded, 16)

        def chunk_view(t):
            flat = t[:, :, :, :].rearrange("p a s c -> p (a s c)").bitcast(F32)
            return flat[:, 0:CHUNK * C].rearrange("p (t c) -> p t c", c=C)

        stat_x = [chunk_view(q_bd), chunk_view(v_bd), chunk_view(k_sb)]
        w_f = sb("w_f", [P, 2 * INNER], F32)
        stats = sb("stats", [P, NCH, GROUPS, 6], F32)
        gn_pv = sb("gn_pv", [P, B, GROUPS, 2], F32)
        gn_mean = sb("gn_mean", [P, B, GROUPS, 2], F32)
        gn_var = sb("gn_var", [P, B, GROUPS, 2], F32)
        gn_dev = sb("gn_dev", [P, B, GROUPS, 2], F32)
        avg = sb("avg", [P, P], F32)
        gn_v = sb("gn_v", [P, B * C], F32)
        gn_s = sb("gn_s", [P, B * C], F32)

        block = ctx.enter_context(nc.Block())

        def row_views(t_dram, row, tile_view):
            both = t_dram[bass.ds(row, 2)]
            for r in range(2):
                yield tile_view[:, 2 * r:2 * r + 2, :], both[r, SHIFT:SHIFT + 2 * L, :].rearrange(
                    "(w t) c -> t w c", w=2)
            n = L - SHIFT
            yield tile_view[0:n, 4:6, :], both[:, SHIFT + 2 * L:W, :].rearrange("r t c -> t r c")
            yield tile_view[n:L, 4:6, :], both[:, 0:SHIFT, :].rearrange("r t c -> t r c")

        ROW_DMAS = 4 * SETS * 16

        def first_rows(eng, step):
            rows = [step * 2 + st * 2 * H for st in range(SETS)]
            return [r if isinstance(r, int) else eng.snap(r) for r in rows]

        def move_step(eng, dram, buf, parity, rows, semaphore, store):
            if not isinstance(rows[0], int):
                apart(eng)
            for st in range(SETS):
                for chip, mem in row_views(dram, rows[st], buf[st * L:(st + 1) * L, parity]):
                    if store:
                        eng.dma_start(mem, chip).then_inc(semaphore, 16)
                    else:
                        eng.dma_start(chip, mem).then_inc(semaphore, 16)

        @block.sync
        def _(sp):
            def load(dst, src):
                sp.dma_start(dst, src).then_inc(w_loaded, 16)

            for half in range(2):
                rows = slice(half * C, (half + 1) * C)
                load(w_f[rows, 0:INNER], wq)
            for half in range(2):
                load(pn_f[half * L:(half + 1) * L, 0], pos.rearrange("a h i j -> i (a h) j"))
                load(pe_f[half * L:(half + 1) * L, 0, 0], wo.rearrange("(s d) c -> d s c", d=DH))
            load(bo_sb[:, :], bo.partition_broadcast(P))
            for ch in range(NCH):
                if ch >= 3:
                    sp.wait_ge(stat_used, ch - 2)
                im, part = ch // CHUNKS, ch % CHUNKS
                src = xflat[im].rearrange("(p t) c -> p t c", p=P)[:, part * CHUNK:(part + 1) * CHUNK, :]
                sp.dma_start(stat_x[ch % 3], src).then_inc(stat_loaded[ch % 3], 16)
                if ch == 2:
                    sp.wait_ge(w_made, 1)
                    for half in range(2):
                        load(w_f[half * C:(half + 1) * C, :], wkv)
            for n in range(2):
                move_step(sp, xrow, x_in, n, first_rows(sp, n), xin_loaded[n], False)
            sp.wait_ge(bd_cleared, 1)

            def q_blocks(tile):
                src = q_sb[:, tile].rearrange("p a (u i) -> p (a u) i", i=L)
                for st in range(SETS):
                    r = slice(st * DH, (st + 1) * DH)
                    sp.dma_start(q_bd[r, tile, :, r], src[r]).then_inc(q_loaded[tile], 16)

            def v_store(parity, tile):
                for w in range(WIN):
                    dst = v_dram[(parity * TILES + tile) * WIN + w].rearrange("a t n -> t a n")
                    sp.dma_start(dst, v_sb[w * L:(w + 1) * L, tile]).then_inc(v_stored[tile], 16)

            def v_blocks(parity, tile):
                for w in range(WIN):
                    r = slice(w * DH, (w + 1) * DH)
                    src = v_dram[(parity * TILES + tile) * WIN + w].rearrange(
                        "a (h t) (s d) -> (t s) (a h) d", h=HEADS, s=SLICES)
                    sp.dma_start(v_bd[r, tile, :, r], src).then_inc(v_loaded[tile], 16)

            sp.wait_ge(ring_free, XT + 8)
            for tile in range(TILES):
                q_blocks(tile)
            for tile in range(TILES):
                sp.wait_ge(ring_free, XT + 8 + 2 * (tile + 1))
                v_store(0, tile)
            sp.wait_ge(v_stored[0], 32)
            v_blocks(0, 0)

            def store_outputs(s):
                rows = first_rows(sp, s.step(-1))
                waits(sp, s, (ring_free, lambda T: out_number(T - 1) + 1))
                move_step(sp, orow, y_sb, 1 - s.step_parity, rows, y_stored[1 - s.step_parity], True)

            def slot(s):
                tt, par = s.tile, s.step_parity
                nxt = 1 - par
                if tt == 0:
                    if s.has(in_slots):
                        waits(sp, s, (v_stored[1], lambda T: 32 * (T // TILES + 1)),
                              (o_filled, lambda T: 2 * (T - 1)))
                        v_blocks(par, 1)
                    if s.has(has_next2):
                        rows = first_rows(sp, s.step(2))
                        waits(sp, s, (xb_made, lambda T: T // TILES + 1),
                              (xc_made, lambda T: T // TILES + 1))
                        move_step(sp, xrow, x_in, par, rows, xin_loaded[par], False)
                    if s.has(has_next):
                        waits(sp, s, (ring_free, lambda T: part_number(T, 7) + 1),
                              (s_filled, lambda T: 2 * (T + 1)))
                        q_blocks(0)
                if tt == 1:
                    if s.has(in_slots):
                        waits(sp, s, (v_stored[2], lambda T: 32 * (T // TILES + 1)),
                              (o_filled, lambda T: 2 * (T - 1)))
                        v_blocks(par, 2)
                    if s.has(has_next):
                        waits(sp, s, (s_filled, lambda T: 2 * (T + 1)))
                        q_blocks(1)
                        for tile in range(TILES):
                            waits(sp, s, (v_loaded[tile], lambda T: 32 * (T // TILES)),
                                  (ring_free, lambda T: part_number(T, 2 * tile + 1) + 1))
                            v_store(nxt, tile)
                if tt == 2:
                    if s.has(has_next):
                        waits(sp, s, (s_filled, lambda T: 2 * (T + 1)))
                        q_blocks(2)
                        waits(sp, s, (v_stored[0], lambda T: 32 * (T // TILES + 2)),
                              (o_filled, lambda T: 2 * (T - 1)))
                        v_blocks(nxt, 0)
                    if s.has(lambda T: TILES < T < SLOTS):
                        store_outputs(s)

            slots(sp, slot)
            store_outputs(Slot(NIT - 1, 8))
            for parity in range(2):
                sp.wait_ge(y_stored[parity], ROW_DMAS * NIT)

        def hi_view(kind, n, par):
            return part_view(kind, n, par, 0)

        def part_view(kind, n, par, part):
            if kind == "q":
                return q_sb[:, :, part, :].rearrange("p a (u s) -> p a u s", s=SLICES)[:, :, :, n]
            if kind == "k":
                return k_sb[:, par, part, :].rearrange("p (u s) -> p u s", s=SLICES)[:, :, n]
            return v_sb[:, n // 2, 2 * part + n % 2, :]

        def o_view(t, hf):
            return t[:, :, :, hf * (L // 2):(hf + 1) * (L // 2)]

        def o_src():
            return o_ps[:, :, :, :].rearrange("p a h (t s) -> p s a (h t)", s=SLICES)

        @block.gpsimd
        def _(pool):
            pool.memset(ident[:, :], 0.0).then_inc(ident_made, 1)
            pool.wait_ge(ident_made, 1)
            pool.affine_select(out=ident[:, :], in_=ident[:, :], compare_op=ALU.not_equal, fill=1.0,
                               base=0, pattern=[[-1, P]], channel_multiplier=1).then_inc(ident_made, 1)
            pool.memset(avg[:, :], 1.0 / P).then_inc(consts_made, 1)
            pool.memset(w_out[:, :, :, :].rearrange("p a s c -> p (a s c)"), 0.0).then_inc(consts_made, 1)
            pool.wait_ge(stat_used, NCH)
            pool.memset(q_bd[:, :, :, :].rearrange("p a s c -> p (a s c)").bitcast(F32), 0.0)
            pool.memset(v_bd[:, :, :, :].rearrange("p a s c -> p (a s c)").bitcast(F32), 0.0).then_inc(bd_cleared, 1)

            def gn_view(pair, what):
                return gn_tab[:, bass.ds(pair, 1), what, :].broadcast_to([P, TILES * WIN, C])

            def center_x(parity, pair):
                pool.tensor_tensor(xc[:, :, :], x_in[:, parity], gn_view(pair, 0), ALU.subtract).then_inc(xc_made, 1)

            def scale_x(pair):
                pool.tensor_tensor(xn[:, :, :], xc[:, :, :], gn_view(pair, 1), ALU.mult).then_inc(xn_made, 1)

            def x_low():
                pool.tensor_tensor(xh[:, :, 1, :], xn[:, :, :], xh[:, :, 0, :], ALU.subtract).then_inc(x_lo_made, 1)

            def add_bias(parity):
                pool.tensor_tensor(x_res[:, parity], x_in[:, parity],
                                   bo_sb[:, None, :].broadcast_to([P, TILES * WIN, C]),
                                   ALU.add).then_inc(xb_made, 1)

            pool.wait_ge(w_loaded, 7 * 16)
            pool.wait_ge(xin_loaded[0], ROW_DMAS)
            add_bias(0)
            pool.wait_ge(gn_made, 3)
            for n in range(2):
                pool.wait_ge(xin_loaded[n], ROW_DMAS)
                pool.wait_ge(x_hi_made, n)
                pool.wait_ge(x_lo_made, n)
                center_x(n, 0)
                pool.wait_ge(xc_made, n + 1)
                scale_x(0)
                pool.wait_ge(x_hi_made, n + 1)
                x_low()

            def half_sums(s, w):
                wait(pool, exp_made, s, lambda T: 2 * T + w + 1)
                wait(pool, sum_made, s, lambda T: 2 * (T - 1) + w + 1)
                e = pe_f[:, s.parity, w]
                pool.tensor_tensor(half_sum[:, w], e[:, :, 0:L // 2], e[:, :, L // 2:L], ALU.add).then_inc(half_made, 1)

            def probabilities(s, w):
                wait(pool, inv_made, s, lambda T: 2 * T + w + 1)
                wait(pool, ph_made, s, lambda T: 2 * (T - 1) + w + 1)
                wait(pool, pl_made, s, lambda T: 2 * (T - 1) + w + 1)
                inv = row_inv[:, s.parity, w, :, None].broadcast_to([P, HEADS, L])
                pool.tensor_tensor(pn_f[:, w], pe_f[:, s.parity, w], inv, ALU.mult).then_inc(norm_made, 1)

            def p_low(s, w):
                wait(pool, ph_made, s, lambda T: 2 * T + w + 1)
                hi = p_hi[:, s.parity, :, w * L:(w + 1) * L]
                lo = p_lo[:, s.parity, :, w * L:(w + 1) * L]
                pool.tensor_tensor(lo, pn_f[:, w], hi, ALU.subtract).then_inc(pl_made, 1)

            def next_center(s):
                wait(pool, xin_loaded[s.step_parity], s, lambda T: ROW_DMAS * ((T // TILES + 2) // 2 + 1))
                wait(pool, x_hi_made, s, lambda T: T // TILES + 2)
                wait(pool, x_lo_made, s, lambda T: T // TILES + 2)
                pair = s.step(2) // (STEPS // 2)
                center_x(s.step_parity, pair)
                wait(pool, xc_made, s, lambda T: T // TILES + 3)
                scale_x(pair)

            def next_x_low(s):
                wait(pool, x_hi_made, s, lambda T: T // TILES + 3)
                x_low()

            def next_bias(s):
                nxt = 1 - s.step_parity
                wait(pool, xin_loaded[nxt], s, lambda T: ROW_DMAS * ((T // TILES + 1) // 2 + 1))
                wait(pool, ring_free, s, lambda T: out_number(T - 1) + 1 if T >= 3 else 0)
                add_bias(nxt)

            def slot(s):
                live = s.has(in_slots)
                before = s.has(lambda T: 1 <= T <= SLOTS)
                next_a = s.tile == 1 and s.has(has_next2)
                next_y = s.tile == 2 and s.has(has_next2)
                next_b = s.tile == 2 and s.has(has_next)
                prev = s.before(1)
                if before:
                    p_low(prev, 1)
                if next_a:
                    next_center(s)
                if next_y:
                    next_x_low(s)
                if live:
                    half_sums(s, 0)
                if next_b:
                    next_bias(s)
                if live:
                    half_sums(s, 1)
                    probabilities(s, 0)
                    probabilities(s, 1)
                    p_low(s, 0)

            slots(pool, slot)

        @block.scalar
        def _(act):
            act.wait_ge(ident_made, 2)
            nc.scalar.activation(ident16[:, :], ident[:, :], ACT.Copy)
            for half in range(2):
                r = slice(half * L, (half + 1) * L)
                last = nc.scalar.activation(pair_up[r, :].rearrange("p (a m) -> p a m", a=2),
                                            ident[r, None, r].broadcast_to([L, 2, L]), ACT.Copy, scale=SIM_UP)
            last.then_inc(w_hi_made, 1)
            act.wait_ge(w_loaded, 7 * 16)
            act.wait_ge(consts_made, 2)
            nc.scalar.activation(w_qkv[:, 0, 0:INNER], w_f[:, 0:INNER], ACT.Copy, scale=W_UP)
            nc.scalar.activation(pos_sb[:, :], pn_f[:, 0].rearrange("p h j -> p (h j)"), ACT.Copy)
            for half in range(2):
                r = slice(half * C, (half + 1) * C)
                last = nc.scalar.activation(w_out[r, 0, :, r], pe_f[r, 0, 0], ACT.Copy, scale=WO_UP)
            last.then_inc(w_hi_made, 1)
            act.wait_ge(w_loaded, 9 * 16)
            nc.scalar.activation(w_qkv[:, 0, INNER:3 * INNER], w_f[:, :], ACT.Copy, scale=W_UP).then_inc(w_hi_made, 1)
            act.wait_ge(gn_step, 5)
            nc.scalar.activation(gn_s[:, :], gn_v[:, :], ACT.Sqrt).then_inc(std_made, 1)

            def hi_part(kind, n, par, ring_bank):
                src = ring[ring_bank]
                if kind == "q":
                    return nc.scalar.activation(hi_view(kind, n, par), src[:, 0:STEP_TOK].rearrange(
                        "p (a u) -> p a u", a=TILES), ACT.Copy)
                if kind == "k":
                    return nc.scalar.activation(hi_view(kind, n, par), src[:, 0:STEP_TOK], ACT.Copy)
                return nc.scalar.activation(hi_view(kind, n, par), src[:, :], ACT.Copy, scale=1.0 / W_UP)

            def x_high():
                nc.scalar.activation(xh[:, :, 0, :], xn[:, :, :], ACT.Copy).then_inc(x_hi_made, 1)

            def stack_x(piece, bank):
                nc.scalar.activation(
                    xs[:, :, piece * 3 * L:(piece + 1) * 3 * L].rearrange("p s (w t) -> p w s t", w=3),
                    ring[bank][:, :].bitcast(F16)[:, 0:3 * P].rearrange("p (w s t) -> p w s t", w=3, s=SETS),
                    ACT.Copy).then_inc(ring_free, 1)

            for n in range(2):
                act.wait_ge(xn_made, n + 1)
                act.wait_ge(ring_filled, n * XT)
                x_high()
                if n == 0:
                    for piece in range(XT):
                        act.wait_ge(ring_filled, piece + 1)
                        stack_x(piece, piece % RING)
            for i, (kind, n) in enumerate(ring_list(0) + ring_list(1) + ring_list(2)):
                act.wait_ge(ring_filled, XT + i + 1)
                hi_part(kind, n, 0, (XT + i) % RING).then_inc(hi_made, 1)
            act.wait_ge(ring_free, XT + PROJ)
            for piece in range(XT):
                act.wait_ge(ring_filled, XT + PROJ + piece + 1)
                stack_x(piece, (XT + PROJ + piece) % RING)

            def exps(s, w):
                wait(act, sub_made, s, lambda T: 2 * T + w + 1)
                wait(act, norm_made, s, lambda T: 2 * (T - 2) + w + 1)
                nc.scalar.activation(pe_f[:, s.parity, w], e_in[:, w], ACT.Exp, scale=1.0 / SIM_UP).then_inc(exp_made, 1)

            def p_high(s, w):
                wait(act, norm_made, s, lambda T: 2 * T + w + 1)
                wait(act, pt_filled, s, lambda T: 2 * (T - 2) + 2)
                nc.scalar.activation(p_hi[:, s.parity, :, w * L:(w + 1) * L], pn_f[:, w], ACT.Copy).then_inc(ph_made, 1)

            def parts(s, lo, hi):
                nxt = 1 - s.step_parity
                for i, (kind, n) in list(enumerate(ring_list(s.tile)))[lo:hi]:
                    if kind == "q" and n == 0:
                        for tile in range(TILES):
                            wait(act, q_loaded[tile], s, lambda T: 32 * (T // TILES + 1))
                    if kind == "k" and n == 0:
                        wait(act, s_filled, s, lambda T: 2 * (T - 1))
                    if kind == "v" and n % 2 == 0:
                        wait(act, v_stored[n // 2], s, lambda T: 32 * (T // TILES + 1))
                    number = lambda T: part_number(T, i)
                    wait(act, ring_filled, s, lambda T: number(T) + 1)
                    hi_part(kind, n, nxt, s.bank(number)).then_inc(hi_made, 1)

            def o_high(s, hf):
                wait(act, o_filled, s, lambda T: 2 * (T - 1) + hf + 1)
                wait(act, ring_filled, s, lambda T: out_number(T) + 1 if T >= 2 else 0)
                nc.scalar.activation(o_view(o_hi, hf), o_src(), ACT.Copy).then_inc(oh_made, 1)

            def transposed(s, bank, dst):
                wait(act, pt_filled, s, lambda T: 2 * (T - 1) + bank + 1)
                wait(act, o_filled, s, lambda T: 2 * (T - 1))
                nc.scalar.activation(dst[:, :, :], pt_ps[bank][:, :, :], ACT.Copy).then_inc(pt_made, 1)

            def next_x_high(s):
                wait(act, xn_made, s, lambda T: T // TILES + 3)
                wait(act, ring_filled, s, lambda T: ring_before(T - 2))
                x_high()

            def next_stack_x(s):
                wait(act, ring_free, s, lambda T: part_number(T, 6))
                for piece in range(XT):
                    wait(act, ring_filled, s, lambda T: part_number(T, 6 + piece) + 1)
                    stack_x(piece, s.bank(lambda T: part_number(T, 6 + piece)))

            def slot(s):
                live = s.has(in_slots)
                ahead = s.has(has_next)
                before = s.has(lambda T: 1 <= T <= SLOTS)
                before2 = s.has(lambda T: 2 <= T <= SLOTS + 1)
                prev = s.before(1)
                if s.tile == 2 and s.has(has_next2):
                    next_x_high(s)
                if before:
                    p_high(prev, 1)
                if ahead:
                    parts(s, 0, 1)
                if before2:
                    o_high(prev, 1)
                if live:
                    exps(s, 0)
                if ahead:
                    parts(s, 1, 3)
                if before:
                    transposed(s, 0, pt_hi)
                if live:
                    exps(s, 1)
                if before:
                    transposed(s, 1, pt_lo)
                if ahead:
                    parts(s, 3, 6)
                if before:
                    o_high(s, 0)
                if ahead:
                    parts(s, 6, 8)
                if live:
                    p_high(s, 0)
                if s.tile == 2 and s.has(has_next2):
                    next_stack_x(s)

            slots(act, slot)

        @block.vector
        def _(dve):
            dve.wait_ge(w_hi_made, 2)
            nc.vector.scalar_tensor_tensor(out=w_qkv[:, 1, 0:INNER], in0=w_f[:, 0:INNER], scalar=W_UP,
                                           in1=w_qkv[:, 0, 0:INNER], op0=ALU.mult, op1=ALU.subtract)
            nc.vector.tensor_tensor(pos_sb[L:P, :], pn_f[L:P, 0].rearrange("p h j -> p (h j)"), pos_sb[L:P, :],
                                    ALU.subtract)
            for half in range(2):
                r = slice(half * C, (half + 1) * C)
                last = nc.vector.scalar_tensor_tensor(out=w_out[r, 1, :, r], in0=pe_f[r, 0, 0], scalar=WO_UP,
                                                      in1=w_out[r, 0, :, r], op0=ALU.mult, op1=ALU.subtract)
            last.then_inc(w_made, 1)
            for ch in range(NCH):
                dve.wait_ge(stat_loaded[ch % 3], 16 * (ch // 3 + 1))
                for g in range(GROUPS):
                    last = nc.vector.bn_stats(stats[:, ch, g, :], stat_x[ch % 3][:, :, 2 * g:2 * g + 2])
                last.then_inc(stat_used, 1)
            dve.wait_ge(stat_used, NCH)
            for im in range(B):
                for g in range(GROUPS):
                    last = nc.vector.bn_aggr(gn_pv[:, im, g, :], stats[:, im * CHUNKS:(im + 1) * CHUNKS, g, :])
            last.then_inc(gn_step, 1)
            dve.wait_ge(gn_step, 1)
            shape = [P, B, GROUPS, 2]
            nc.vector.tensor_copy(gn_mean[:, :, :, :], gn_pv[:, :, :, 0:1].broadcast_to(shape))
            nc.vector.tensor_copy(gn_var[:, :, :, :], gn_pv[:, :, :, 1:2].broadcast_to(shape)).then_inc(gn_step, 1)
            dve.wait_ge(w_hi_made, 3)
            nc.vector.scalar_tensor_tensor(out=w_qkv[:, 1, INNER:3 * INNER], in0=w_f[:, :], scalar=W_UP,
                                           in1=w_qkv[:, 0, INNER:3 * INNER], op0=ALU.mult,
                                           op1=ALU.subtract).then_inc(w_made, 1)
            dve.wait_ge(gn_sums, 1)
            flat = lambda t: t[:, :, :, :].rearrange("p b g e -> p (b g e)")
            halves = [(slice(st * L, (st + 1) * L), slice(2 * st * C, 2 * (st + 1) * C)) for st in range(SETS)]
            pairs = lambda v: v.rearrange("p (i c) -> p i c", c=C)
            for r, images in halves:
                nc.vector.tensor_copy(gn_tab[r, :, 0, :], pairs(ring[0][r, images]))
            nc.vector.tensor_tensor(flat(gn_dev), flat(gn_mean), ring[0][:, 0:B * C], ALU.subtract).then_inc(gn_step, 1)
            dve.wait_ge(gn_step, 3)
            nc.vector.tensor_tensor(flat(gn_mean), flat(gn_dev), flat(gn_dev), ALU.mult).then_inc(gn_made, 1)
            dve.wait_ge(gn_made, 1)
            nc.vector.tensor_tensor(flat(gn_dev), flat(gn_mean), flat(gn_var), ALU.add).then_inc(gn_step, 1)
            dve.wait_ge(gn_sums, 2)
            nc.vector.tensor_scalar(gn_v[:, :], ring[1][:, 0:B * C], GN_EPS, None, ALU.add).then_inc(gn_step, 1)
            dve.wait_ge(std_made, 1)
            nc.vector.reciprocal(gn_v[:, :], gn_s[:, :]).then_inc(gn_made, 1)
            dve.wait_ge(gn_made, 2)
            for r, images in halves:
                last = nc.vector.tensor_copy(gn_tab[r, :, 1, :], pairs(gn_v[r, images]))
            last.then_inc(gn_made, 1)

            def low_part(kind, n, par, bank):
                src = ring[bank]
                hi, lo = part_view(kind, n, par, 0), part_view(kind, n, par, 1)
                if kind == "q":
                    src = src[:, 0:STEP_TOK].rearrange("p (a u) -> p a u", a=TILES)
                    ins = nc.vector.tensor_tensor(lo, src, hi, ALU.subtract)
                elif kind == "k":
                    ins = nc.vector.tensor_tensor(lo, src[:, 0:STEP_TOK], hi, ALU.subtract)
                else:
                    ins = nc.vector.scalar_tensor_tensor(out=lo, in0=src[:, :], scalar=1.0 / W_UP, in1=hi,
                                                         op0=ALU.mult, op1=ALU.subtract)
                ins.then_inc(ring_free, 1)

            for i, (kind, n) in enumerate(ring_list(0) + ring_list(1) + ring_list(2)):
                dve.wait_ge(hi_made, i + 1)
                low_part(kind, n, 0, (XT + i) % RING)

            def maxima(s, w):
                wait(dve, s_filled, s, lambda T: 2 * T + w + 1)
                nc.vector.reduce_max(row_max[:, w], s_ps[w][:, :, :], AX.X).then_inc(max_made, 1)

            def below_max(s, w):
                wait(dve, max_made, s, lambda T: 2 * T + w + 1)
                wait(dve, exp_made, s, lambda T: 2 * (T - 1) + w + 1)
                nc.vector.tensor_tensor(e_in[:, w], s_ps[w][:, :, :], row_max[:, w, :, None].broadcast_to(
                    [P, HEADS, L]), ALU.subtract).then_inc(sub_made, 1)

            def sums(s, w):
                wait(dve, half_made, s, lambda T: 2 * T + w + 1)
                nc.vector.reduce_sum(row_sum[:, w], half_sum[:, w], AX.X).then_inc(sum_made, 1)

            def scaled(s, w):
                wait(dve, sum_made, s, lambda T: 2 * T + w + 1)
                nc.vector.tensor_scalar(row_sum_s[:, w], row_sum[:, w], 1.0 / P_UP, None,
                                        ALU.mult).then_inc(sum_scaled, 1)

            def inverse(s, w):
                wait(dve, sum_scaled, s, lambda T: 2 * T + w + 1)
                nc.vector.reciprocal(row_inv[:, s.parity, w], row_sum_s[:, w]).then_inc(inv_made, 1)

            def parts(s, lo, hi):
                for i, (kind, n) in list(enumerate(ring_list(s.tile)))[lo:hi]:
                    wait(dve, hi_made, s, lambda T: parts_before(T) + i + 1)
                    low_part(kind, n, 1 - s.step_parity, s.bank(lambda T: part_number(T, i)))

            def o_low(s, hf):
                wait(dve, oh_made, s, lambda T: 2 * (T - 1) + hf + 1)
                nc.vector.tensor_tensor(o_view(o_lo, hf), o_src(), o_view(o_hi, hf), ALU.subtract).then_inc(ol_made, 1)

            def finish(s):
                tile = (s.u - 2) % TILES
                par = ((s.u - 2) // TILES) % 2
                wait(dve, ring_filled, s, lambda T: out_number(T) + 1)
                wait(dve, xb_made, s, lambda T: (T - 2) // TILES + 1)
                if tile == 0:
                    wait(dve, y_stored[par], s, lambda T: ROW_DMAS * ((T - 2) // TILES // 2))
                nc.vector.scalar_tensor_tensor(
                    out=y_sb[:, par, 2 * tile:2 * tile + 2, :].rearrange("p w c -> p (w c)"),
                    in0=ring[s.bank(out_number)][:, 0:P], scalar=OUT_DOWN,
                    in1=x_res[:, par, 2 * tile:2 * tile + 2, :].rearrange("p w c -> p (w c)"),
                    op0=ALU.mult, op1=ALU.add).then_inc(ring_free, 1)

            def slot(s):
                live = s.has(in_slots)
                ahead = s.has(has_next)
                before = s.has(lambda T: 1 <= T <= SLOTS)
                before2 = s.has(lambda T: 2 <= T <= SLOTS + 1)
                prev = s.before(1)
                if live:
                    maxima(s, 0)
                    below_max(s, 0)
                if ahead:
                    parts(s, 0, 1)
                if live:
                    maxima(s, 1)
                if before2:
                    o_low(prev, 1)
                if live:
                    below_max(s, 1)
                if ahead:
                    parts(s, 1, 3)
                if live:
                    sums(s, 0)
                if s.has(lambda T: T >= 2):
                    finish(s)
                if live:
                    scaled(s, 0)
                    sums(s, 1)
                    inverse(s, 0)
                if ahead:
                    parts(s, 3, 5)
                if live:
                    scaled(s, 1)
                if ahead:
                    parts(s, 5, 6)
                if live:
                    inverse(s, 1)
                if before:
                    o_low(s, 0)
                if ahead:
                    parts(s, 6, 8)

            slots(dve, slot)

        @block.tensor
        def _(pe):
            mm = nc.tensor.matmul
            pe.wait_ge(consts_made, 1)
            for number, (t, bank) in enumerate(((gn_mean, 0), (gn_dev, 1))):
                pe.wait_ge(gn_step, 2 + 2 * number)
                mm(ring[bank][:, 0:B * C], avg[:, :], t[:, :, :, :].rearrange("p b g e -> p (b g e)"),
                   start=True, stop=True).then_inc(gn_sums, 1)

            def transpose_x(piece, bank):
                for j in range(3):
                    last = nc.tensor.transpose(ring[bank][:, :].bitcast(F16)[:, j * P:(j + 1) * P],
                                               xh[:, 3 * piece + j].rearrange("p a c -> p (a c)"), ident16[:, :])
                last.then_inc(ring_filled, 1)

            def project(kind, n, bank):
                if kind == "v":
                    tile, st = n // 2, n % 2
                    for part in range(2):
                        last = mm(ring[bank][:, :], xs[:, st, tile * P:(tile + 1) * P],
                                  w_qkv[:, part, 2 * INNER:3 * INNER], start=part == 0, stop=part == 1)
                else:
                    col = (INNER if kind == "k" else 0) + n * DH
                    for part in range(2):
                        for st in range(SETS):
                            last = mm(ring[bank][st * DH:(st + 1) * DH, 0:STEP_TOK],
                                      w_qkv[:, part, col:col + DH], xs[:, st, :],
                                      start=part == 0, stop=part == 1)
                last.then_inc(ring_filled, 1)

            pe.wait_ge(gn_made, 3)
            pe.wait_ge(w_hi_made, 1)
            pe.wait_ge(x_lo_made, 1)
            for piece in range(XT):
                transpose_x(piece, piece % RING)
            pe.wait_ge(w_made, 2)
            pe.wait_ge(ring_free, XT)
            for i, (kind, n) in enumerate(ring_list(0) + ring_list(1) + ring_list(2)):
                pe.wait_ge(ring_free, max(XT, XT + i - RING + 1))
                project(kind, n, (XT + i) % RING)
            pe.wait_ge(x_lo_made, 2)
            for piece in range(XT):
                pe.wait_ge(ring_free, XT + PROJ + piece - RING + 1)
                transpose_x(piece, (XT + PROJ + piece) % RING)

            def scores(s, w):
                if w == 0:
                    wait(pe, q_loaded[s.tile], s, lambda T: 32 * (T // TILES + 1))
                    wait(pe, ring_free, s, k_results)
                wait(pe, sub_made, s, lambda T: 2 * (T - 1) + w + 1)
                bank = s_ps[w]
                mm(bank[:, :, :].rearrange("p h j -> p (h j)"), pair_up[:, :], pos_sb[:, :], start=True, stop=False)
                for h in range(HEADS):
                    u = w * HEADS + h
                    key = (s.tile * U + u) * L
                    for qp, kp in ((0, 0), (0, 1), (1, 0)):
                        last = mm(bank[:, h, :], q_bd[:, s.tile, qp * U + u, :],
                                  k_sb[:, s.step_parity, kp, key:key + L], start=False,
                                  stop=h == HEADS - 1 and qp == 1)
                last.then_inc(s_filled, 1)

            def output(s):
                wait(pe, ol_made, s, lambda T: 2 * (T - 2) + 2)
                wait(pe, ring_free, s, lambda T: out_number(T) - RING + 1)
                bank = ring[s.bank(out_number)]
                for sl in range(SLICES):
                    for i, (o, part) in enumerate(((o_hi, 0), (o_hi, 1), (o_lo, 0))):
                        last = mm(bank[:, 0:P], o[:, sl].rearrange("p a t -> p (a t)"), w_out[:, part, sl, :],
                                  start=sl == 0 and i == 0, stop=sl == SLICES - 1 and i == 2)
                last.then_inc(ring_filled, 1)

            def parts(s, lo, hi):
                for i, (kind, n) in list(enumerate(ring_list(s.tile)))[lo:hi]:
                    if s.tile == 0 and i == 0:
                        wait(pe, ring_free, s, lambda T: ring_before(T))
                    wait(pe, ring_free, s, lambda T: part_number(T, i) - RING + 1)
                    project(kind, n, s.bank(lambda T: part_number(T, i)))

            def transpose_p(s, part):
                par = (s.u - 1) % 2
                wait(pe, pl_made, s, lambda T: 2 * (T - 1) + 2)
                wait(pe, pt_made, s, lambda T: 2 * (T - 2) + part + 1)
                for h in range(HEADS):
                    last = nc.tensor.transpose(pt_ps[part][:, h, :], (p_hi, p_lo)[part][:, par, h, :], ident16[:, :])
                last.then_inc(pt_filled, 1)

            def weigh(s, hf):
                tile = (s.u - 1) % TILES
                if hf == 0:
                    wait(pe, pt_made, s, lambda T: 2 * T)
                    wait(pe, v_loaded[tile], s, lambda T: 32 * ((T - 1) // TILES + 1))
                wait(pe, ol_made, s, lambda T: 2 * (T - 1) + hf)
                for st in range(SETS):
                    for h4 in range(HEADS // 2):
                        h = hf * (HEADS // 2) + h4
                        for i, (vp, p) in enumerate(((0, pt_hi), (0, pt_lo), (1, pt_hi))):
                            last = mm(o_ps[:, st, h4, :], v_bd[:, tile, (2 * vp + st) * HEADS + h, :],
                                      p[:, h, st * L:(st + 1) * L], start=i == 0, stop=i == 2)
                last.then_inc(o_filled, 1)

            def next_transpose_x(s):
                wait(pe, x_lo_made, s, lambda T: T // TILES + 3)
                for piece in range(XT):
                    wait(pe, ring_free, s, lambda T: part_number(T, 6 + piece) - RING + 1)
                    transpose_x(piece, s.bank(lambda T: part_number(T, 6 + piece)))

            def slot(s):
                live = s.has(in_slots)
                ahead = s.has(has_next)
                before = s.has(lambda T: 1 <= T <= SLOTS)
                before2 = s.has(lambda T: 2 <= T <= SLOTS + 1)
                prev = s.before(1)
                if live:
                    scores(s, 0)
                if before2:
                    weigh(prev, 1)
                if ahead:
                    parts(s, 0, 1)
                if live:
                    scores(s, 1)
                if ahead:
                    parts(s, 1, 3)
                if before:
                    transpose_p(s, 0)
                    transpose_p(s, 1)
                if s.has(lambda T: T >= 2):
                    output(s)
                if ahead:
                    parts(s, 3, 6)
                if before:
                    weigh(s, 0)
                if ahead:
                    parts(s, 6, 8)
                if s.tile == 2 and s.has(has_next2):
                    next_transpose_x(s)

            slots(pe, slot)


_INS = ["x", "L0_conv_Wq", "L0_conv_Wkv", "L0_conv_Wo", "L0_conv_bo", "L0_conv_pos_emb"]


def kernel(**inputs):
    import numpy as _np
    import concourse.bacc as _bacc
    from concourse import mybir as _mybir
    from concourse.bass_utils import run_bass_kernel_spmd as _run

    nc = _bacc.Bacc("TRN2", target_bir_lowering=False, num_devices=1)
    arrays, args = {}, []
    for name in _INS:
        a = _np.ascontiguousarray(inputs[name])
        arrays[f"in_{name}_dram"] = a
        args.append(nc.dram_tensor(f"in_{name}_dram", a.shape, _mybir.dt.from_np(a.dtype), kind="ExternalInput").ap())
    shape = arrays["in_x_dram"].shape
    args.append(nc.dram_tensor("out_0_dram", shape, _mybir.dt.float32, kind="ExternalOutput").ap())
    build(nc, *args)
    r = _run(nc, [arrays], core_ids=[0])
    return r.results[0]["out_0_dram"]
```
